# Optimizing a Trainium2 kernel written in Bass

```python
import numpy as np
import jax
import jax.numpy as jnp

def _softmax(x, axis=-1):
    return jax.nn.softmax(x, axis=axis)

def _gelu(x):
    return jax.nn.gelu(x, approximate=True)

def _silu(x):
    return jax.nn.silu(x)

def _sigmoid(x):
    return jax.nn.sigmoid(x)

def _layernorm(x, axis=-1, eps=1e-05):
    m = jnp.mean(x, axis=axis, keepdims=True)
    v = jnp.var(x, axis=axis, keepdims=True)
    return (x - m) / jnp.sqrt(v + eps)

def _scatter_add(tgt, idx, src, axis=0):
    return tgt.at[idx].add(src)

def _segment_sum(src, seg, n):
    return jax.ops.segment_sum(src, seg, n)
kernel_name = 'mk_dlrm_tower_d1_rec_r8_4ed4d6'

def setup_inputs(seed: int=0):
    np.random.seed(seed)
    _w = jnp.asarray

    def _rec_inputs():
        import jax
        import jax.numpy as jnp
        _tk = jax.random.key(seed)
        ids = jnp.stack([jax.random.randint(jax.random.fold_in(_tk, 200 + f), (2048,), 0, v, jnp.int32) for f, v in enumerate([12500, 1000, 1250, 1000, 1000, 1000, 1000, 12500, 12500, 125000, 1000, 1250, 1000, 12500, 1000, 1250, 1000, 1000, 12500, 12500, 1000, 12500, 12500, 1000, 1250, 1000])], axis=1)
        tbl_0 = 0.05 * jax.random.normal(jax.random.fold_in(_tk, 500 + 0), (12500, 128), jnp.float32)
        tbl_1 = 0.05 * jax.random.normal(jax.random.fold_in(_tk, 500 + 1), (1000, 128), jnp.float32)
        tbl_2 = 0.05 * jax.random.normal(jax.random.fold_in(_tk, 500 + 2), (1250, 128), jnp.float32)
        tbl_3 = 0.05 * jax.random.normal(jax.random.fold_in(_tk, 500 + 3), (1000, 128), jnp.float32)
        tbl_4 = 0.05 * jax.random.normal(jax.random.fold_in(_tk, 500 + 4), (1000, 128), jnp.float32)
        tbl_5 = 0.05 * jax.random.normal(jax.random.fold_in(_tk, 500 + 5), (1000, 128), jnp.float32)
        tbl_6 = 0.05 * jax.random.normal(jax.random.fold_in(_tk, 500 + 6), (1000, 128), jnp.float32)
        tbl_7 = 0.05 * jax.random.normal(jax.random.fold_in(_tk, 500 + 7), (12500, 128), jnp.float32)
        tbl_8 = 0.05 * jax.random.normal(jax.random.fold_in(_tk, 500 + 8), (12500, 128), jnp.float32)
        tbl_9 = 0.05 * jax.random.normal(jax.random.fold_in(_tk, 500 + 9), (125000, 128), jnp.float32)
        tbl_10 = 0.05 * jax.random.normal(jax.random.fold_in(_tk, 500 + 10), (1000, 128), jnp.float32)
        tbl_11 = 0.05 * jax.random.normal(jax.random.fold_in(_tk, 500 + 11), (1250, 128), jnp.float32)
        tbl_12 = 0.05 * jax.random.normal(jax.random.fold_in(_tk, 500 + 12), (1000, 128), jnp.float32)
        tbl_13 = 0.05 * jax.random.normal(jax.random.fold_in(_tk, 500 + 13), (12500, 128), jnp.float32)
        tbl_14 = 0.05 * jax.random.normal(jax.random.fold_in(_tk, 500 + 14), (1000, 128), jnp.float32)
        tbl_15 = 0.05 * jax.random.normal(jax.random.fold_in(_tk, 500 + 15), (1250, 128), jnp.float32)
        tbl_16 = 0.05 * jax.random.normal(jax.random.fold_in(_tk, 500 + 16), (1000, 128), jnp.float32)
        tbl_17 = 0.05 * jax.random.normal(jax.random.fold_in(_tk, 500 + 17), (1000, 128), jnp.float32)
        tbl_18 = 0.05 * jax.random.normal(jax.random.fold_in(_tk, 500 + 18), (12500, 128), jnp.float32)
        tbl_19 = 0.05 * jax.random.normal(jax.random.fold_in(_tk, 500 + 19), (12500, 128), jnp.float32)
        tbl_20 = 0.05 * jax.random.normal(jax.random.fold_in(_tk, 500 + 20), (1000, 128), jnp.float32)
        tbl_21 = 0.05 * jax.random.normal(jax.random.fold_in(_tk, 500 + 21), (12500, 128), jnp.float32)
        tbl_22 = 0.05 * jax.random.normal(jax.random.fold_in(_tk, 500 + 22), (12500, 128), jnp.float32)
        tbl_23 = 0.05 * jax.random.normal(jax.random.fold_in(_tk, 500 + 23), (1000, 128), jnp.float32)
        tbl_24 = 0.05 * jax.random.normal(jax.random.fold_in(_tk, 500 + 24), (1250, 128), jnp.float32)
        tbl_25 = 0.05 * jax.random.normal(jax.random.fold_in(_tk, 500 + 25), (1000, 128), jnp.float32)
        _rk = jax.random.fold_in(_tk, 7)
        r_dense_features = -0.000520686 + 1.00062 * jax.random.normal(jax.random.fold_in(_rk, 101), (2048, 128), jnp.float32)
        W_top1 = 0.0405887 * jax.random.normal(jax.random.fold_in(_tk, 801), (607, 512), jnp.float32)
        W_top2 = 0.0441942 * jax.random.normal(jax.random.fold_in(_tk, 802), (512, 256), jnp.float32)
        W_top3 = 0.0625 * jax.random.normal(jax.random.fold_in(_tk, 803), (256, 1), jnp.float32)
        b_top1 = jnp.zeros((512,), jnp.float32)
        b_top2 = jnp.zeros((256,), jnp.float32)
        return (r_dense_features, ids, tbl_0, tbl_1, tbl_2, tbl_3, tbl_4, tbl_5, tbl_6, tbl_7, tbl_8, tbl_9, tbl_10, tbl_11, tbl_12, tbl_13, tbl_14, tbl_15, tbl_16, tbl_17, tbl_18, tbl_19, tbl_20, tbl_21, tbl_22, tbl_23, tbl_24, tbl_25, W_top1, b_top1, W_top2, b_top2, W_top3)
    r_dense_features, ids, tbl_0, tbl_1, tbl_2, tbl_3, tbl_4, tbl_5, tbl_6, tbl_7, tbl_8, tbl_9, tbl_10, tbl_11, tbl_12, tbl_13, tbl_14, tbl_15, tbl_16, tbl_17, tbl_18, tbl_19, tbl_20, tbl_21, tbl_22, tbl_23, tbl_24, tbl_25, W_top1, b_top1, W_top2, b_top2, W_top3 = _rec_inputs()

    def _L0_rec_setup():
        import jax, jax.numpy as jnp
        import numpy as np
        B, F, D = (2048, 26, 128)
        key = jax.random.key(seed)
        k1, k2 = jax.random.split(key)
        dense_features = jax.random.normal(k1, (B, D), dtype=jnp.float32)
        sparse_values = jax.random.normal(k2, (B, F, D), dtype=jnp.float32)
        return {'dense_features': dense_features, 'sparse_values': sparse_values}
    _L0_rec_all = _L0_rec_setup()
    _L0_rec_in = {k: v for k, v in _L0_rec_all.items() if k in ()}
    del _L0_rec_all
    return {'r_dense_features': r_dense_features, 'ids': ids, 'tbl_0': tbl_0, 'tbl_1': tbl_1, 'tbl_2': tbl_2, 'tbl_3': tbl_3, 'tbl_4': tbl_4, 'tbl_5': tbl_5, 'tbl_6': tbl_6, 'tbl_7': tbl_7, 'tbl_8': tbl_8, 'tbl_9': tbl_9, 'tbl_10': tbl_10, 'tbl_11': tbl_11, 'tbl_12': tbl_12, 'tbl_13': tbl_13, 'tbl_14': tbl_14, 'tbl_15': tbl_15, 'tbl_16': tbl_16, 'tbl_17': tbl_17, 'tbl_18': tbl_18, 'tbl_19': tbl_19, 'tbl_20': tbl_20, 'tbl_21': tbl_21, 'tbl_22': tbl_22, 'tbl_23': tbl_23, 'tbl_24': tbl_24, 'tbl_25': tbl_25, 'W_top1': W_top1, 'b_top1': b_top1, 'W_top2': W_top2, 'b_top2': b_top2, 'W_top3': W_top3}

def reference(r_dense_features, ids, tbl_0, tbl_1, tbl_2, tbl_3, tbl_4, tbl_5, tbl_6, tbl_7, tbl_8, tbl_9, tbl_10, tbl_11, tbl_12, tbl_13, tbl_14, tbl_15, tbl_16, tbl_17, tbl_18, tbl_19, tbl_20, tbl_21, tbl_22, tbl_23, tbl_24, tbl_25, W_top1, b_top1, W_top2, b_top2, W_top3):
    import jax
    import jax.numpy as jnp

    def _L0_rec_ref(dense_features, sparse_values):
        import jax, jax.numpy as jnp
        import numpy as np
        B, F, D = (2048, 26, 128)
        sd = jnp.einsum('bfd,bd->bf', sparse_values, dense_features)
        ss = jnp.einsum('bfd,bgd->bfg', sparse_values, sparse_values)
        iu, ju = jnp.triu_indices(F, k=1)
        pairs = ss[:, iu, ju]
        return jnp.concatenate([dense_features, sd, pairs], axis=1)
    e = jnp.stack([tbl_0[ids[:, 0]], tbl_1[ids[:, 1]], tbl_2[ids[:, 2]], tbl_3[ids[:, 3]], tbl_4[ids[:, 4]], tbl_5[ids[:, 5]], tbl_6[ids[:, 6]], tbl_7[ids[:, 7]], tbl_8[ids[:, 8]], tbl_9[ids[:, 9]], tbl_10[ids[:, 10]], tbl_11[ids[:, 11]], tbl_12[ids[:, 12]], tbl_13[ids[:, 13]], tbl_14[ids[:, 14]], tbl_15[ids[:, 15]], tbl_16[ids[:, 16]], tbl_17[ids[:, 17]], tbl_18[ids[:, 18]], tbl_19[ids[:, 19]], tbl_20[ids[:, 20]], tbl_21[ids[:, 21]], tbl_22[ids[:, 22]], tbl_23[ids[:, 23]], tbl_24[ids[:, 24]], tbl_25[ids[:, 25]]], axis=1)
    z = _L0_rec_ref(r_dense_features, e)
    z = z.reshape(z.shape[0], -1)
    h = jnp.concatenate([z, r_dense_features], axis=1)
    h = jnp.maximum(h @ W_top1 + b_top1, 0.0)
    h = jnp.maximum(h @ W_top2 + b_top2, 0.0)
    y = h @ W_top3
    return y

_drawn_inputs = setup_inputs


def setup_inputs(seed=0):
    import zlib

    import numpy as np

    out = dict(_drawn_inputs(seed))
    spreads = {'b_top1': (0.0, 0.1), 'b_top2': (0.0, 0.1)}
    factors = {}
    for name, (base, spread) in spreads.items():
        noise = np.random.default_rng([zlib.crc32(name.encode()), seed]).standard_normal(out[name].shape)
        drawn = base * np.exp(spread * noise) if base else spread * noise
        out[name] = jnp.asarray(drawn.astype(out[name].dtype))
    for name, factor in factors.items():
        out[name] = (out[name] * factor).astype(out[name].dtype)
    return out
```

```python
from contextlib import ExitStack

import concourse.bass as bass
from concourse import mybir

B, F, D = 2048, 26, 128
H1, H2 = 512, 256
NPAIR = F * (F - 1) // 2
ONE_HOT = (1, 3, 4, 5, 6, 10)
ROWS = 1000
GATHERED = tuple(f for f in range(F) if f not in ONE_HOT)
NO, NG = len(ONE_HOT), len(GATHERED)
CH = 256
NCH = B // CH
TILES = CH // 128
GROUPS = CH // 4
FW = F + 1
KT = 8
KP = ROWS // KT
SPLIT = KP // 16 * 16

OH_SLOTS = NO // 2
TR_SLOTS = NG // 2
SLOTS = OH_SLOTS + TR_SLOTS
OH_AT = tuple(1 + 4 * i for i in range(OH_SLOTS))
TR_AT = tuple(j for j in range(SLOTS) if j not in OH_AT)
STEPS = 16
G_BANKS = 4
G_GROUPS = GROUPS // G_BANKS
A_BANKS = -(-F // 4)
Z_TILES = ((0, 128), (128, 128), (256, F + NPAIR - 256))
A_USES = A_BANKS + len(Z_TILES)
Z_STEP = A_BANKS + 1
L1_STEP = Z_STEP + len(Z_TILES)
L2_STEP = L1_STEP + 3
M_USES = 4


def pair_offset(i):
    return F + i * (F - 1) - i * (i - 1) // 2


def wait(eng, sem, value):
    if not isinstance(value, int) or value > 0:
        eng.wait_ge(sem, value)


def dlrm_tower(nc, dense_t, ids_gather, ids_one_hot, tables, w1, b1, w2, b2, w3, out):
    f32, f32r, i32 = mybir.dt.float32, mybir.dt.float32r, mybir.dt.int32
    ALU, ACT = mybir.AluOpType, mybir.ActivationFunctionType
    ctx = ExitStack()
    with ctx:
        def sb(name, shape, dt=f32):
            return ctx.enter_context(nc.sbuf_tensor(name, shape, dt))

        def banks(name, n):
            return [ctx.enter_context(nc.psum_tensor(f"{name}{i}", [128, 512], f32)) for i in range(n)]

        def sem(name):
            return ctx.enter_context(nc.semaphore(name))

        ident = sb("ident", [128, 128])
        first_row = sb("first_row", [128, 1])
        table = sb("table", [128, KT, D])
        table_hi = sb("table_hi", [128, NO, KT, D], f32r)
        table_lo = sb("table_lo", [128, NO, KT, D], f32r)
        idx = [sb(f"idx{i}", [128, TILES * NG], i32) for i in range(2)]
        rows = sb("rows", [128, TR_SLOTS, 2, TILES, D])
        idb = [sb(f"idb{i}", [128, NO, CH], i32) for i in range(2)]
        one_hot = [sb(f"one_hot{i}", [128, KT, CH], f32r) for i in range(2)]
        xt = sb("xt", [128, B])
        et = [sb(f"et{i}", [128, CH * FW + 32 - FW]) for i in range(2)]
        gram = [sb(f"gram{i}", [128, GROUPS * F]) for i in range(2)]
        z = sb("z", [128, 4, F + NPAIR])
        zt = sb("zt", [128, len(Z_TILES), CH])
        h1 = sb("h1", [128, H1 // 128, CH])
        h2 = sb("h2", [128, H2 // 128, CH])
        y = [sb(f"y{i}", [1, CH]) for i in range(2)]
        w1x = sb("w1x", [128, H1])
        w1x2 = sb("w1x2", [128, H1])
        w1z = sb("w1z", [128, len(Z_TILES), H1])
        w2s = sb("w2s", [128, H1 // 128, H2])
        w3s = sb("w3s", [128, H2 // 128])
        b1s = sb("b1s", [128, H1 // 128])
        b2s = sb("b2s", [128, H2 // 128])

        et_ps = banks("et_ps", 2)
        g_ps = banks("g_ps", 2)
        a_ps = banks("a_ps", 2)
        m_ps = banks("m_ps", 2)

        idx_in = [sem(f"idx_in{i}") for i in range(2)]
        idb_in = [sem(f"idb_in{i}") for i in range(2)]
        table_in = sem("table_in")
        xt_in = sem("xt_in")
        w_in = sem("w_in")
        consts = sem("consts")
        table_split = sem("table_split")
        table_read = sem("table_read")
        w_ready = sem("w_ready")
        rows_in = [sem(f"rows_in{j}") for j in range(TR_SLOTS)]
        oh_ready = sem("oh_ready")
        oh_used = sem("oh_used")
        et_done = sem("et_done")
        et_copied = sem("et_copied")
        xt_copied = sem("xt_copied")
        g_done = sem("g_done")
        g_copied = sem("g_copied")
        a_done = sem("a_done")
        a_free = sem("a_free")
        m_done = sem("m_done")
        m_free = sem("m_free")
        y_out = [sem(f"y_out{i}") for i in range(2)]

        y_free = sem("y_free")
        waits_apart = sem("waits_apart")

        block = ctx.enter_context(nc.Block())

        def apart(eng):
            eng.sem_inc(waits_apart, 1)

        def phases(eng, phase):
            for p in range(2):
                phase(p, p)
            with eng.Fori(1, NCH // 2) as pair:
                phase(2 * pair, 0)
                phase(2 * pair + 1, 1)
            for p in range(NCH, NCH + 2):
                phase(p, p % 2)

        def lookup(p):
            return not isinstance(p, int) or p < NCH

        def grams(p):
            return not isinstance(p, int) or 1 <= p <= NCH

        def mlp(p):
            return not isinstance(p, int) or p >= 2

        @block.sync
        def _(sp):
            def load_ids(p, par):
                wait(sp, et_done, (p - 2) * SLOTS + TR_AT[-1] + 1)
                sp.dma_start(idx[par][:, :], ids_gather[bass.ds(p, 1), :, :].rearrange("a p n -> (a p) n"))\
                    .then_inc(idx_in[par], 16)
                wait(sp, oh_ready, (p - 1) * NO)
                sp.dma_start(idb[par][:, :, :],
                             ids_one_hot[bass.ds(p, 1), :, :].broadcast_to([128, NO, CH]))\
                    .then_inc(idb_in[par], 16)

            def store(p, par):
                wait(sp, m_free, (p + 1) * M_USES + 2)
                sp.dma_start(out[bass.ds(p, 1), :], y[par][:, :]).then_inc(y_out[par], 16)
                wait(sp, y_out[par], (p - par) * 8 + 16)
                sp.sem_inc(y_free, 1)

            load_ids(0, 0)
            load_ids(1, 1)
            for n, f in enumerate(ONE_HOT):
                wait(sp, table_read, 2 * n)
                src = tables[f].rearrange("(p k) d -> p k d", k=KT)
                sp.dma_start(table[0:SPLIT, :, :], src[0:SPLIT]).then_inc(table_in, 16)
                sp.dma_start(table[SPLIT:KP, :, :], src[SPLIT:KP]).then_inc(table_in, 16)
            with sp.Fori(1, NCH // 2) as pair:
                load_ids(2 * pair, 0)
                load_ids(2 * pair + 1, 1)
                store(2 * pair - 2, 0)
                store(2 * pair - 1, 1)
            for p in range(NCH - 2, NCH):
                store(p, p % 2)

        @block.gpsimd
        def _(pool):
            nc.gpsimd.memset(ident[:, :], 0.0).then_inc(consts, 1)
            nc.gpsimd.iota(first_row[:, :], [[0, 1]], base=0, channel_multiplier=KT,
                           allow_small_or_imprecise_dtypes=True).then_inc(consts, 1)
            for t in et:
                nc.gpsimd.memset(t[:, CH * FW:], 0.0).then_inc(consts, 1)
            pool.wait_ge(consts, 4)
            nc.gpsimd.affine_select(out=ident[:, :], in_=ident[:, :], compare_op=ALU.not_equal, fill=1.0,
                                    base=0, pattern=[[-1, 128]], channel_multiplier=1).then_inc(consts, 1)

            def gathers(p, par):
                wait(pool, idx_in[par], (p - par) * 8 + 16)
                for j in range(TR_SLOTS):
                    wait(pool, et_done, (p - 1) * SLOTS + TR_AT[j] + 1)
                    apart(pool)
                    for n in range(2):
                        for t in range(TILES):
                            k = 2 * j + n
                            i = t * NG + k
                            nc.gpsimd.indirect_dma_start(
                                out=rows[:, j, n, t, :], out_offset=None, in_=tables[GATHERED[k]],
                                in_offset=bass.IndirectOffsetOnAxis(idx[par][:, i:i + 1], 0))\
                                .then_inc(rows_in[j], 16)

            gathers(0, 0)
            gathers(1, 1)
            with pool.Fori(1, NCH // 2) as pair:
                gathers(2 * pair, 0)
                gathers(2 * pair + 1, 1)

        @block.scalar
        def _(act):
            act.sem_inc(m_free, 2)
            act.sem_inc(y_free, 2)
            act.dma_start(xt[:, :], dense_t).then_inc(xt_in, 16)
            act.dma_start(w1x[:, :], w1[0:D, :]).then_inc(w_in, 16)
            act.dma_start(w1x2[:, :], w1[D + F + NPAIR:, :]).then_inc(w_in, 16)
            for k, (at, n) in enumerate(Z_TILES):
                act.dma_start(w1z[0:n, k, :], w1[D + at:D + at + n, :]).then_inc(w_in, 16)
            act.dma_start(w2s[:, :, :], w2.rearrange("(k p) n -> p k n", p=128)).then_inc(w_in, 16)
            act.dma_start(w3s[:, :], w3).then_inc(w_in, 16)
            act.dma_start(b1s[:, :], b1).then_inc(w_in, 16)
            act.dma_start(b2s[:, :], b2).then_inc(w_in, 16)
            act.wait_ge(xt_in, 16)
            act.wait_ge(w_in, 16 * 9)

            def phase(p, par):
                if lookup(p):
                    wait(act, g_done, (p - 1) * G_BANKS)
                    e3 = et[par][:, 0:CH * FW].rearrange("d (b f) -> d b f", f=FW)
                    nc.scalar.copy(e3[:, :, F], xt[:, bass.ds(p * CH, CH)]).then_inc(xt_copied, 1)
                for s in range(STEPS):
                    if grams(p) and s % 4 == 3:
                        bank = s // 4
                        wait(act, g_done, (p - 1) * G_BANKS + bank + 1)
                        n = G_GROUPS * F
                        nc.scalar.copy(gram[1 - par][:, bank * n:(bank + 1) * n], g_ps[bank % 2][:, 0:n])\
                            .then_inc(g_copied, 1)
                    if mlp(p):
                        m0 = (p - 2) * M_USES
                        if s in (L1_STEP, L1_STEP + 1):
                            u = s - L1_STEP
                            wait(act, m_done, m0 + u + 1)
                            for n in range(2):
                                m = 2 * u + n
                                last = nc.scalar.activation(h1[:, m, :], m_ps[u][:, n * CH:(n + 1) * CH], ACT.Relu,
                                                            bias=b1s[:, m:m + 1])
                            last.then_inc(m_free, 1)
                        if s == L2_STEP:
                            wait(act, m_done, m0 + 3)
                            for m in range(2):
                                last = nc.scalar.activation(h2[:, m, :], m_ps[0][:, m * CH:(m + 1) * CH], ACT.Relu,
                                                            bias=b2s[:, m:m + 1])
                            last.then_inc(m_free, 1)
                    if lookup(p) and s < SLOTS:
                        wait(act, et_done, p * SLOTS + s + 1)
                        fs = [GATHERED[2 * TR_AT.index(s) + n] if s in TR_AT else ONE_HOT[2 * OH_AT.index(s) + n]
                              for n in range(2)]
                        dst = e3[:, :, fs[0]:fs[1] + 1:fs[1] - fs[0]].rearrange("d b f -> d f b")
                        src = et_ps[(par * SLOTS + s) % 2][:, :].rearrange("d (f b) -> d f b", f=2)
                        nc.scalar.copy(dst, src).then_inc(et_copied, 1)
                if mlp(p):
                    wait(act, m_done, (p - 2) * M_USES + 4)
                    wait(act, y_free, p - 2 + 1)
                    nc.scalar.copy(y[par][:, :], m_ps[1][0:1, 0:CH]).then_inc(m_free, 1)

            phases(act, phase)

        @block.vector
        def _(dve):
            dve.sem_inc(a_free, 2)
            dve.wait_ge(w_in, 16 * 9)
            nc.vector.tensor_tensor(w1x[:, :], w1x[:, :], w1x2[:, :], ALU.add).then_inc(w_ready, 1)
            for n in range(NO):
                dve.wait_ge(table_in, 32 * (n + 1))
                nc.vector.tensor_copy(table_hi[0:KP, n], table[0:KP]).then_inc(table_read, 1)
                dve.wait_ge(table_read, 2 * n + 1)
                nc.vector.tensor_tensor(table_lo[0:KP, n], table[0:KP], table_hi[0:KP, n].bitcast(f32),
                                        ALU.subtract).then_inc(table_read, 1)
            dve.wait_ge(consts, 5)

            def build(p, par, n):
                i = n // 2
                if n % 2 == 0:
                    wait(dve, oh_used, p * OH_SLOTS + i)
                else:
                    wait(dve, et_done, (p * SLOTS + OH_AT[i - 1] if i else (p - 1) * SLOTS + OH_AT[-1]) + 1)
                for k in range(KT):
                    last = nc.vector.tensor_scalar(one_hot[n % 2][0:KP, k, :], idb[par][0:KP, n, :],
                                                   first_row[0:KP, 0:1], float(k), ALU.subtract, ALU.is_equal)
                last.then_inc(oh_ready, 1)

            def phase(p, par):
                if lookup(p):
                    wait(dve, idb_in[par], (p - par) * 8 + 16)
                for s in range(STEPS):
                    if mlp(p):
                        a0 = (p - 2) * A_USES
                        if s < A_BANKS:
                            wait(dve, a_done, a0 + s + 1)
                            cols = min(4, F - 4 * s)
                            ps = a_ps[s % 2][0:GROUPS, 0:cols * 128].rearrange("g (i q f) -> g i q f", i=cols, q=4)
                            for i in range(4 * s, 4 * s + cols):
                                if i < F - 1:
                                    at = pair_offset(i)
                                    nc.vector.tensor_copy(z[0:GROUPS, :, at:at + F - 1 - i], ps[:, i % 4, :, i + 1:F])
                            nc.vector.tensor_copy(z[0:GROUPS, :, 4 * s:4 * s + cols].rearrange("g q i -> g i q"),
                                                  ps[:, :, :, F]).then_inc(a_free, 1)
                        if Z_STEP <= s < L1_STEP:
                            u = s - Z_STEP
                            n = Z_TILES[u][1]
                            wait(dve, a_done, a0 + A_BANKS + u + 1)
                            nc.vector.tensor_copy(zt[0:n, u, :].rearrange("z (g q) -> z q g", q=4),
                                                  a_ps[(A_BANKS + u) % 2][0:n, 0:CH].rearrange("z (q g) -> z q g", q=4))\
                                .then_inc(a_free, 1)
                    if lookup(p) and s in OH_AT:
                        i = OH_AT.index(s)
                        build(p, par, 2 * i)
                        build(p, par, 2 * i + 1)

            phases(dve, phase)

        @block.tensor
        def _(pe):
            pe.wait_ge(consts, 5)
            pe.wait_ge(w_ready, 1)

            def phase(p, par):
                for s in range(STEPS):
                    if grams(p):
                        bank = s // 4
                        if s == 0:
                            wait(pe, et_copied, p * SLOTS)
                            wait(pe, xt_copied, p)
                        if s % 4 == 0:
                            wait(pe, g_copied, (p - 1) * G_BANKS + bank - 1)
                        e = et[1 - par]
                        for grp in range(s * GROUPS // STEPS, (s + 1) * GROUPS // STEPS):
                            for q in range(4):
                                b, c = (4 * grp + q) * FW, grp % G_GROUPS * F
                                last = nc.tensor.matmul(g_ps[bank % 2][32 * q:32 * q + 32, c:c + F], e[:, b:b + 32],
                                                        e[:, b:b + F], start=True, stop=True)
                        if s % 4 == 3:
                            last.then_inc(g_done, 1)
                    if mlp(p):
                        a0 = (p - 2) * A_USES
                        if s < A_BANKS:
                            if s == 0:
                                wait(pe, g_copied, (p - 1) * G_BANKS)
                            wait(pe, a_free, a0 + s + 1)
                            apart(pe)
                            for i in range(4 * s, min(4 * s + 4, F)):
                                last = nc.tensor.transpose(a_ps[s % 2][0:GROUPS, i % 4 * 128:i % 4 * 128 + 128],
                                                           gram[par][:, i:GROUPS * F:F], ident[:, :])
                            last.then_inc(a_done, 1)
                        if Z_STEP <= s < L1_STEP:
                            u = s - Z_STEP
                            at, n = Z_TILES[u]
                            wait(pe, a_free, a0 + A_BANKS + max(u + 1, 2))
                            apart(pe)
                            for q in range(4):
                                last = nc.tensor.transpose(a_ps[(A_BANKS + u) % 2][0:n, q * GROUPS:(q + 1) * GROUPS],
                                                           z[0:GROUPS, q, at:at + n], ident[0:GROUPS, 0:GROUPS])
                            last.then_inc(a_done, 1)
                        m0 = (p - 2) * M_USES
                        if s in (L1_STEP, L1_STEP + 1):
                            u = s - L1_STEP
                            wait(pe, m_free, m0 + u + 1)
                            wait(pe, a_free, a0 + A_BANKS + len(Z_TILES) + 2)
                            for n in range(2):
                                m = 2 * u + n
                                dst = m_ps[u][:, n * CH:(n + 1) * CH]
                                nc.tensor.matmul(dst, w1x[:, m * 128:(m + 1) * 128], xt[:, bass.ds((p - 2) * CH, CH)],
                                                 start=True, stop=False)
                                for k, (_, rows_k) in enumerate(Z_TILES):
                                    last = nc.tensor.matmul(dst, w1z[0:rows_k, k, m * 128:(m + 1) * 128],
                                                            zt[0:rows_k, k, :], start=False, stop=k == len(Z_TILES) - 1)
                            last.then_inc(m_done, 1)
                        if s == L2_STEP:
                            wait(pe, m_free, m0 + 2 + 2)
                            for m in range(2):
                                for k in range(4):
                                    last = nc.tensor.matmul(m_ps[0][:, m * CH:(m + 1) * CH],
                                                            w2s[:, k, m * 128:(m + 1) * 128], h1[:, k, :],
                                                            start=k == 0, stop=k == 3)
                            last.then_inc(m_done, 1)
                    if lookup(p) and s < SLOTS:
                        ps = et_ps[(par * SLOTS + s) % 2]
                        wait(pe, et_copied, p * SLOTS + s - 1)
                        if s in TR_AT:
                            j = TR_AT.index(s)
                            wait(pe, rows_in[j], (p + 1) * 16 * 2 * TILES)
                            for n in range(2):
                                for t in range(TILES):
                                    last = nc.tensor.transpose(ps[:, n * CH + t * 128:n * CH + (t + 1) * 128],
                                                               rows[:, j, n, t, :], ident[:, :])
                            last.then_inc(et_done, 1)
                        else:
                            for n in range(2):
                                i = 2 * OH_AT.index(s) + n
                                oh = one_hot[n]
                                wait(pe, oh_ready, p * NO + i + 1)
                                for k in range(KT):
                                    for part in (table_hi, table_lo):
                                        last = nc.tensor.matmul(ps[:, n * CH:(n + 1) * CH], part[0:KP, i, k, :],
                                                                oh[0:KP, k, :], start=k == 0 and part is table_hi,
                                                                stop=k == KT - 1 and part is table_lo)
                                last.then_inc((oh_used, et_done)[n], 1)
                if mlp(p):
                    wait(pe, m_free, (p - 2) * M_USES + 3 + 2)
                    for k in range(2):
                        last = nc.tensor.matmul(m_ps[1][0:1, 0:CH], w3s[:, k:k + 1], h2[:, k, :],
                                                start=k == 0, stop=k == 1)
                    last.then_inc(m_done, 1)

            phases(pe, phase)


def kernel(**inputs):
    import numpy as np
    import concourse.bacc as bacc
    from concourse.bass_utils import run_bass_kernel_spmd

    nc = bacc.Bacc("TRN2", target_bir_lowering=False, num_devices=1)
    arrays = {}

    def give(name, a):
        a = np.ascontiguousarray(a)
        arrays[name] = a
        return nc.dram_tensor(name, a.shape, mybir.dt.from_np(a.dtype), kind="ExternalInput").ap()

    ids = np.asarray(inputs["ids"])
    gather = ids[:, list(GATHERED)].reshape(NCH, TILES, 128, NG).transpose(0, 2, 1, 3).reshape(NCH, 128, TILES * NG)
    one_hot = ids[:, list(ONE_HOT)].reshape(NCH, CH, NO).transpose(0, 2, 1)
    args = [
        give("dense_t", np.asarray(inputs["r_dense_features"]).T),
        give("ids_gather", gather),
        give("ids_one_hot", one_hot),
        [give(f"tbl_{f}_in", np.asarray(inputs[f"tbl_{f}"])) for f in range(F)],
        give("w1", np.asarray(inputs["W_top1"])),
        give("b1", np.asarray(inputs["b_top1"]).reshape(H1 // 128, 128).T),
        give("w2", np.asarray(inputs["W_top2"])),
        give("b2", np.asarray(inputs["b_top2"]).reshape(H2 // 128, 128).T),
        give("w3", np.asarray(inputs["W_top3"]).reshape(H2 // 128, 128).T),
    ]
    out = nc.dram_tensor("out", (NCH, CH), mybir.dt.float32, kind="ExternalOutput").ap()
    dlrm_tower(nc, *args, out)
    r = run_bass_kernel_spmd(nc, [arrays], core_ids=[0])
    return r.results[0]["out"].reshape(B, 1)
```

```python
from contextlib import ExitStack

import concourse.bass as bass
from concourse import mybir

B, F, D = 2048, 26, 128
H1, H2 = 512, 256
NPAIR = F * (F - 1) // 2
ONE_HOT = (1, 3, 4, 5, 6, 10)
ROWS = 1000
GATHERED = tuple(f for f in range(F) if f not in ONE_HOT)
NO, NG = len(ONE_HOT), len(GATHERED)
CH = 256
NCH = B // CH
TILES = CH // 128
GROUPS = CH // 4
FW = F + 1
KT = 8
KP = ROWS // KT
SPLIT = KP // 16 * 16

OH_SLOTS = NO // 2
TR_SLOTS = NG // 2
SLOTS = OH_SLOTS + TR_SLOTS
OH_AT = tuple(1 + 4 * i for i in range(OH_SLOTS))
TR_AT = tuple(j for j in range(SLOTS) if j not in OH_AT)
STEPS = 16
ROW_RING = 5
ROUNDS = TR_SLOTS // ROW_RING
G_BANKS = 4
G_GROUPS = GROUPS // G_BANKS
A_BANKS = -(-F // 4)
Z_TILES = ((0, 128), (128, 128), (256, F + NPAIR - 256))
A_USES = A_BANKS + len(Z_TILES)
Z_STEP = A_BANKS + 1
L1_STEP = Z_STEP + len(Z_TILES)
L2_STEP = L1_STEP + 3
M_USES = 4


def pair_offset(i):
    return F + i * (F - 1) - i * (i - 1) // 2


def wait(eng, sem, value):
    if not isinstance(value, int) or value > 0:
        eng.wait_ge(sem, value)


def dlrm_tower(nc, dense_t, ids_gather, ids_one_hot, tables, w1, b1, w2, b2, w3, out):
    f32, f32r, i32 = mybir.dt.float32, mybir.dt.float32r, mybir.dt.int32
    ALU, ACT = mybir.AluOpType, mybir.ActivationFunctionType
    ctx = ExitStack()
    with ctx:
        def sb(name, shape, dt=f32):
            return ctx.enter_context(nc.sbuf_tensor(name, shape, dt))

        def banks(name, n):
            return [ctx.enter_context(nc.psum_tensor(f"{name}{i}", [128, 512], f32)) for i in range(n)]

        def sem(name):
            return ctx.enter_context(nc.semaphore(name))

        ident = sb("ident", [128, 128])
        first_row = sb("first_row", [128, 1])
        table_hi = sb("table_hi", [128, NO, KT, D], f32r)
        table_lo = sb("table_lo", [128, NO, KT, D], f32r)
        idx = [sb(f"idx{i}", [128, TILES * NG], i32) for i in range(2)]
        rows = sb("rows", [128, ROW_RING, 2, TILES, D])
        idb = sb("idb", [128, OH_SLOTS, 2, CH], i32)
        one_hot = [sb(f"one_hot{i}", [128, KT, CH], f32r) for i in range(2)]
        xt = sb("xt", [128, B])
        et = [sb(f"et{i}", [128, CH * FW + 32 - FW]) for i in range(2)]
        gram = [sb(f"gram{i}", [128, GROUPS * F]) for i in range(2)]
        table = [g[:, 0:KT * D].rearrange("p (k d) -> p k d", k=KT) for g in gram]
        z = sb("z", [128, 4, F + NPAIR])
        zt = sb("zt", [128, len(Z_TILES), CH])
        w1x2 = zt[:, 0:2, :]
        h1 = sb("h1", [128, H1 // 128, CH])
        h2 = sb("h2", [128, H2 // 128, CH])
        y = sb("y", [128, B // 128])
        w1x = sb("w1x", [128, H1])
        w1z = sb("w1z", [128, len(Z_TILES), H1])
        w2s = sb("w2s", [128, H1 // 128, H2])
        w3s = sb("w3s", [128, H2 // 128])
        b1s = sb("b1s", [128, H1 // 128])
        b2s = sb("b2s", [128, H2 // 128])

        et_ps = banks("et_ps", 2)
        g_ps = banks("g_ps", 2)
        a_ps = banks("a_ps", 2)
        m_ps = banks("m_ps", 2)

        idx_in = [sem(f"idx_in{i}") for i in range(2)]
        idb_in = [sem(f"idb_in{i}") for i in range(OH_SLOTS)]
        table_in = [sem(f"table_in{i}") for i in range(2)]
        xt_in = sem("xt_in")
        w_in = sem("w_in")
        consts = sem("consts")
        table_split = sem("table_split")
        table_read = sem("table_read")
        w_ready = sem("w_ready")
        rows_in = [sem(f"rows_in{j}") for j in range(ROW_RING)]
        oh_ready = sem("oh_ready")
        oh_used = sem("oh_used")
        et_done = sem("et_done")
        et_copied = sem("et_copied")
        xt_copied = sem("xt_copied")
        g_done = sem("g_done")
        g_copied = sem("g_copied")
        a_done = sem("a_done")
        a_free = sem("a_free")
        m_done = sem("m_done")
        m_free = sem("m_free")
        y_out = sem("y_out")

        waits_apart = sem("waits_apart")

        block = ctx.enter_context(nc.Block())

        def apart(eng):
            eng.sem_inc(waits_apart, 1)

        def phases(eng, phase):
            for p in range(2):
                phase(p, p)
            with eng.Fori(1, NCH // 2) as pair:
                phase(2 * pair, 0)
                phase(2 * pair + 1, 1)
            for p in range(NCH, NCH + 2):
                phase(p, p % 2)

        def lookup(p):
            return not isinstance(p, int) or p < NCH

        def grams(p):
            return not isinstance(p, int) or 1 <= p <= NCH

        def mlp(p):
            return not isinstance(p, int) or p >= 2

        @block.sync
        def _(sp):
            def load_indices(p, par):
                wait(sp, et_done, (p - 2) * SLOTS + TR_AT[-1] + 1)
                sp.dma_start(idx[par][:, :], ids_gather[bass.ds(p, 1), :, :].rearrange("a p n -> (a p) n"))\
                    .then_inc(idx_in[par], 16)

            def load_ids(p):
                for i in range(OH_SLOTS):
                    wait(sp, oh_ready, (p - 1) * NO + 2 * i + 2)
                    src = ids_one_hot[bass.ds(p, 1), 2 * i:2 * i + 2, :]
                    sp.dma_start(idb[:, i, :, :], src.broadcast_to([128, 2, CH])).then_inc(idb_in[i], 16)

            load_indices(0, 0)
            for n, f in enumerate(ONE_HOT):
                if n == 2:
                    load_ids(0)
                wait(sp, table_read, 2 * (n - 1))
                src = tables[f].rearrange("(p k) d -> p k d", k=KT)
                sp.dma_start(table[n % 2][0:SPLIT], src[0:SPLIT]).then_inc(table_in[n % 2], 16)
                sp.dma_start(table[n % 2][SPLIT:KP], src[SPLIT:KP]).then_inc(table_in[n % 2], 16)
            load_indices(1, 1)
            load_ids(1)
            with sp.Fori(1, NCH // 2) as pair:
                for par in range(2):
                    load_indices(2 * pair + par, par)
                    load_ids(2 * pair + par)
            sp.wait_ge(m_free, NCH * M_USES + 2)
            sp.dma_start(out, y[:, :]).then_inc(y_out, 16)
            sp.wait_ge(y_out, 16)

        @block.gpsimd
        def _(pool):
            nc.gpsimd.memset(ident[:, :], 0.0).then_inc(consts, 1)
            nc.gpsimd.iota(first_row[:, :], [[0, 1]], base=0, channel_multiplier=KT,
                           allow_small_or_imprecise_dtypes=True).then_inc(consts, 1)
            for t in et:
                nc.gpsimd.memset(t[:, CH * FW:], 0.0).then_inc(consts, 1)
            pool.wait_ge(consts, 4)
            nc.gpsimd.affine_select(out=ident[:, :], in_=ident[:, :], compare_op=ALU.not_equal, fill=1.0,
                                    base=0, pattern=[[-1, 128]], channel_multiplier=1).then_inc(consts, 1)

            def gathers(p, par):
                wait(pool, idx_in[par], (p - par) * 8 + 16)
                for j in range(TR_SLOTS):
                    r = j % ROW_RING
                    wait(pool, et_done, p * SLOTS + TR_AT[j - ROW_RING] + 1 - (SLOTS if j < ROW_RING else 0))
                    apart(pool)
                    for n in range(2):
                        for t in range(TILES):
                            k = 2 * j + n
                            i = t * NG + k
                            nc.gpsimd.indirect_dma_start(
                                out=rows[:, r, n, t, :], out_offset=None, in_=tables[GATHERED[k]],
                                in_offset=bass.IndirectOffsetOnAxis(idx[par][:, i:i + 1], 0))\
                                .then_inc(rows_in[r], 16)

            gathers(0, 0)
            gathers(1, 1)
            with pool.Fori(1, NCH // 2) as pair:
                gathers(2 * pair, 0)
                gathers(2 * pair + 1, 1)

        @block.scalar
        def _(act):
            act.sem_inc(m_free, 2)
            act.dma_start(xt[:, :], dense_t).then_inc(xt_in, 16)
            act.dma_start(w1x[:, :], w1[0:D, :]).then_inc(w_in, 16)
            act.dma_start(w1x2.rearrange("p a b -> p (a b)"), w1[D + F + NPAIR:, :]).then_inc(w_in, 16)
            for k, (at, n) in enumerate(Z_TILES):
                act.dma_start(w1z[0:n, k, :], w1[D + at:D + at + n, :]).then_inc(w_in, 16)
            act.dma_start(w2s[:, :, :], w2.rearrange("(k p) n -> p k n", p=128)).then_inc(w_in, 16)
            act.dma_start(w3s[:, :], w3).then_inc(w_in, 16)
            act.dma_start(b1s[:, :], b1).then_inc(w_in, 16)
            act.dma_start(b2s[:, :], b2).then_inc(w_in, 16)
            act.wait_ge(xt_in, 16)
            act.wait_ge(w_in, 16 * 9)

            def phase(p, par):
                if lookup(p):
                    wait(act, g_done, (p - 1) * G_BANKS)
                    e3 = et[par][:, 0:CH * FW].rearrange("d (b f) -> d b f", f=FW)
                    nc.scalar.copy(e3[:, :, F], xt[:, bass.ds(p * CH, CH)]).then_inc(xt_copied, 1)
                for s in range(STEPS):
                    if grams(p) and s % 4 == 3:
                        bank = s // 4
                        wait(act, g_done, (p - 1) * G_BANKS + bank + 1)
                        n = G_GROUPS * F
                        nc.scalar.copy(gram[1 - par][:, bank * n:(bank + 1) * n], g_ps[bank % 2][:, 0:n])\
                            .then_inc(g_copied, 1)
                    if mlp(p):
                        m0 = (p - 2) * M_USES
                        if s in (L1_STEP, L1_STEP + 1):
                            u = s - L1_STEP
                            wait(act, m_done, m0 + u + 1)
                            for n in range(2):
                                m = 2 * u + n
                                last = nc.scalar.activation(h1[:, m, :], m_ps[u][:, n * CH:(n + 1) * CH], ACT.Relu,
                                                            bias=b1s[:, m:m + 1])
                            last.then_inc(m_free, 1)
                        if s == L2_STEP:
                            wait(act, m_done, m0 + 3)
                            for m in range(2):
                                last = nc.scalar.activation(h2[:, m, :], m_ps[0][:, m * CH:(m + 1) * CH], ACT.Relu,
                                                            bias=b2s[:, m:m + 1])
                            last.then_inc(m_free, 1)
                    if lookup(p) and s < SLOTS:
                        wait(act, et_done, p * SLOTS + s + 1)
                        fs = [GATHERED[2 * TR_AT.index(s) + n] if s in TR_AT else ONE_HOT[2 * OH_AT.index(s) + n]
                              for n in range(2)]
                        dst = e3[:, :, fs[0]:fs[1] + 1:fs[1] - fs[0]].rearrange("d b f -> d f b")
                        src = et_ps[(par * SLOTS + s) % 2][:, :].rearrange("d (f b) -> d f b", f=2)
                        nc.scalar.copy(dst, src).then_inc(et_copied, 1)
                if mlp(p):
                    wait(act, m_done, (p - 2) * M_USES + 4)
                    nc.scalar.copy(y[:, bass.ds((p - 2) * TILES, TILES)], m_ps[1][:, 0:TILES]).then_inc(m_free, 1)

            phases(act, phase)

        @block.vector
        def _(dve):
            dve.sem_inc(a_free, 2)
            def split(n):
                dve.wait_ge(table_in[n % 2], 32 * (n // 2 + 1))
                nc.vector.tensor_copy(table_hi[0:KP, n], table[n % 2][0:KP]).then_inc(table_read, 1)
                dve.wait_ge(table_read, 2 * n + 1)
                nc.vector.tensor_tensor(table_lo[0:KP, n], table[n % 2][0:KP], table_hi[0:KP, n].bitcast(f32),
                                        ALU.subtract).then_inc(table_read, 1)

            dve.wait_ge(consts, 5)

            def build_slot(p, i):
                if isinstance(p, int) and p == 0:
                    split(2 * i)
                    split(2 * i + 1)
                wait(dve, idb_in[i], (p + 1) * 16)
                build(p, 2 * i)
                build(p, 2 * i + 1)

            def build(p, n):
                i = n // 2
                if n % 2 == 0:
                    wait(dve, oh_used, p * OH_SLOTS + i)
                else:
                    wait(dve, et_done, (p * SLOTS + OH_AT[i - 1] if i else (p - 1) * SLOTS + OH_AT[-1]) + 1)
                for k in range(KT):
                    last = nc.vector.tensor_scalar(one_hot[n % 2][0:KP, k, :], idb[0:KP, n // 2, n % 2, :],
                                                   first_row[0:KP, 0:1], float(k), ALU.subtract, ALU.is_equal)
                last.then_inc(oh_ready, 1)

            def phase(p, par):
                if isinstance(p, int) and p == 1:
                    dve.wait_ge(w_in, 16 * 9)
                    nc.vector.tensor_tensor(w1x[:, :], w1x[:, :], w1x2.rearrange("p a b -> p (a b)"), ALU.add).then_inc(w_ready, 1)
                if lookup(p):
                    build_slot(p, 0)
                for s in range(STEPS):
                    if mlp(p):
                        a0 = (p - 2) * A_USES
                        if s < A_BANKS:
                            wait(dve, a_done, a0 + s + 1)
                            cols = min(4, F - 4 * s)
                            ps = a_ps[s % 2][0:GROUPS, 0:cols * 128].rearrange("g (i q f) -> g i q f", i=cols, q=4)
                            for i in range(4 * s, 4 * s + cols):
                                if i < F - 1:
                                    at = pair_offset(i)
                                    nc.vector.tensor_copy(z[0:GROUPS, :, at:at + F - 1 - i], ps[:, i % 4, :, i + 1:F])
                            nc.vector.tensor_copy(z[0:GROUPS, :, 4 * s:4 * s + cols].rearrange("g q i -> g i q"),
                                                  ps[:, :, :, F]).then_inc(a_free, 1)
                        if Z_STEP <= s < L1_STEP:
                            u = s - Z_STEP
                            n = Z_TILES[u][1]
                            wait(dve, a_done, a0 + A_BANKS + u + 1)
                            nc.vector.tensor_copy(zt[0:n, u, :].rearrange("z (g q) -> z q g", q=4),
                                                  a_ps[(A_BANKS + u) % 2][0:n, 0:CH].rearrange("z (q g) -> z q g", q=4))\
                                .then_inc(a_free, 1)
                    if lookup(p) and s in OH_AT[:-1]:
                        build_slot(p, OH_AT.index(s) + 1)

            phases(dve, phase)

        @block.tensor
        def _(pe):
            pe.wait_ge(consts, 5)

            def phase(p, par):
                for s in range(STEPS):
                    if grams(p):
                        bank = s // 4
                        if s == 0:
                            wait(pe, et_copied, p * SLOTS)
                            wait(pe, xt_copied, p)
                        if s % 4 == 0:
                            wait(pe, g_copied, (p - 1) * G_BANKS + bank - 1)
                        e = et[1 - par]
                        for grp in range(s * GROUPS // STEPS, (s + 1) * GROUPS // STEPS):
                            for q in range(4):
                                b, c = (4 * grp + q) * FW, grp % G_GROUPS * F
                                last = nc.tensor.matmul(g_ps[bank % 2][32 * q:32 * q + 32, c:c + F], e[:, b:b + 32],
                                                        e[:, b:b + F], start=True, stop=True)
                        if s % 4 == 3:
                            last.then_inc(g_done, 1)
                    if mlp(p):
                        a0 = (p - 2) * A_USES
                        if s < A_BANKS:
                            if s == 0:
                                wait(pe, g_copied, (p - 1) * G_BANKS)
                            wait(pe, a_free, a0 + s + 1)
                            apart(pe)
                            for i in range(4 * s, min(4 * s + 4, F)):
                                last = nc.tensor.transpose(a_ps[s % 2][0:GROUPS, i % 4 * 128:i % 4 * 128 + 128],
                                                           gram[par][:, i:GROUPS * F:F], ident[:, :])
                            last.then_inc(a_done, 1)
                        if Z_STEP <= s < L1_STEP:
                            u = s - Z_STEP
                            at, n = Z_TILES[u]
                            wait(pe, a_free, a0 + A_BANKS + max(u + 1, 2))
                            apart(pe)
                            for q in range(4):
                                last = nc.tensor.transpose(a_ps[(A_BANKS + u) % 2][0:n, q * GROUPS:(q + 1) * GROUPS],
                                                           z[0:GROUPS, q, at:at + n], ident[0:GROUPS, 0:GROUPS])
                            last.then_inc(a_done, 1)
                        m0 = (p - 2) * M_USES
                        if isinstance(p, int) and p == 2 and s == L1_STEP:
                            pe.wait_ge(w_ready, 1)
                        if s in (L1_STEP, L1_STEP + 1):
                            u = s - L1_STEP
                            wait(pe, m_free, m0 + u + 1)
                            wait(pe, a_free, a0 + A_BANKS + len(Z_TILES) + 2)
                            for n in range(2):
                                m = 2 * u + n
                                dst = m_ps[u][:, n * CH:(n + 1) * CH]
                                nc.tensor.matmul(dst, w1x[:, m * 128:(m + 1) * 128], xt[:, bass.ds((p - 2) * CH, CH)],
                                                 start=True, stop=False)
                                for k, (_, rows_k) in enumerate(Z_TILES):
                                    last = nc.tensor.matmul(dst, w1z[0:rows_k, k, m * 128:(m + 1) * 128],
                                                            zt[0:rows_k, k, :], start=False, stop=k == len(Z_TILES) - 1)
                            last.then_inc(m_done, 1)
                        if s == L2_STEP:
                            wait(pe, m_free, m0 + 2 + 2)
                            for m in range(2):
                                for k in range(4):
                                    last = nc.tensor.matmul(m_ps[0][:, m * CH:(m + 1) * CH],
                                                            w2s[:, k, m * 128:(m + 1) * 128], h1[:, k, :],
                                                            start=k == 0, stop=k == 3)
                            last.then_inc(m_done, 1)
                    if lookup(p) and s < SLOTS:
                        ps = et_ps[(par * SLOTS + s) % 2]
                        wait(pe, et_copied, p * SLOTS + s - 1)
                        if s in TR_AT:
                            j = TR_AT.index(s)
                            r = j % ROW_RING
                            wait(pe, rows_in[r], (p * ROUNDS + j // ROW_RING + 1) * 16 * 2 * TILES)
                            for n in range(2):
                                for t in range(TILES):
                                    last = nc.tensor.transpose(ps[:, n * CH + t * 128:n * CH + (t + 1) * 128],
                                                               rows[:, r, n, t, :], ident[:, :])
                            last.then_inc(et_done, 1)
                        else:
                            for n in range(2):
                                i = 2 * OH_AT.index(s) + n
                                oh = one_hot[n]
                                wait(pe, oh_ready, p * NO + i + 1)
                                for k in range(KT):
                                    for part in (table_hi, table_lo):
                                        last = nc.tensor.matmul(ps[:, n * CH:(n + 1) * CH], part[0:KP, i, k, :],
                                                                oh[0:KP, k, :], start=k == 0 and part is table_hi,
                                                                stop=k == KT - 1 and part is table_lo)
                                last.then_inc((oh_used, et_done)[n], 1)
                if mlp(p):
                    wait(pe, m_free, (p - 2) * M_USES + 3 + 2)
                    for t in range(TILES):
                        for k in range(2):
                            last = nc.tensor.matmul(m_ps[1][:, t:t + 1], h2[:, k, t * 128:(t + 1) * 128],
                                                    w3s[:, k:k + 1], start=k == 0, stop=k == 1)
                    last.then_inc(m_done, 1)

            phases(pe, phase)


def kernel(**inputs):
    import numpy as np
    import concourse.bacc as bacc
    from concourse.bass_utils import run_bass_kernel_spmd

    nc = bacc.Bacc("TRN2", target_bir_lowering=False, num_devices=1)
    arrays = {}

    def give(name, a):
        a = np.ascontiguousarray(a)
        arrays[name] = a
        return nc.dram_tensor(name, a.shape, mybir.dt.from_np(a.dtype), kind="ExternalInput").ap()

    ids = np.asarray(inputs["ids"])
    gather = ids[:, list(GATHERED)].reshape(NCH, TILES, 128, NG).transpose(0, 2, 1, 3).reshape(NCH, 128, TILES * NG)
    one_hot = ids[:, list(ONE_HOT)].reshape(NCH, CH, NO).transpose(0, 2, 1)
    args = [
        give("dense_t", np.asarray(inputs["r_dense_features"]).T),
        give("ids_gather", gather),
        give("ids_one_hot", one_hot),
        [give(f"tbl_{f}_in", np.asarray(inputs[f"tbl_{f}"])) for f in range(F)],
        give("w1", np.asarray(inputs["W_top1"])),
        give("b1", np.asarray(inputs["b_top1"]).reshape(H1 // 128, 128).T),
        give("w2", np.asarray(inputs["W_top2"])),
        give("b2", np.asarray(inputs["b_top2"]).reshape(H2 // 128, 128).T),
        give("w3", np.asarray(inputs["W_top3"]).reshape(H2 // 128, 128).T),
    ]
    out = nc.dram_tensor("out", (128, B // 128), mybir.dt.float32, kind="ExternalOutput").ap()
    dlrm_tower(nc, *args, out)
    r = run_bass_kernel_spmd(nc, [arrays], core_ids=[0])
    return r.results[0]["out"].T.reshape(B, 1)
```

```python
from contextlib import ExitStack
from itertools import accumulate

import concourse.bass as bass
from concourse import mybir

B, F, D = 2048, 26, 128
H1, H2 = 512, 256
NPAIR = F * (F - 1) // 2
ONE_HOT = (1, 3, 4, 5, 6, 10, 12, 14)
ROWS = 1000
GATHERED = tuple(f for f in range(F) if f not in ONE_HOT)
NO, NG = len(ONE_HOT), len(GATHERED)
COLUMNS = GATHERED + ONE_HOT
CH = 256
NCH = B // CH
TILES = CH // 128
GROUPS = CH // 4
FW = F + 1
KT = 8
KP = ROWS // KT
SPLIT = KP // 16 * 16

SCHEDULE = [(step[0], int(step[1:])) for step in (
    "O0 B2 G4 O1 B3 G5 T0 G6 O2 B4 G7 O3 B5 A0 T1 A1 O4 O5 A2 T2 A3 T3 Z0 Z1 T4 T5 Z2 B6 B7 L0 T6 L1 T7 "
    "O6 O7 T8 L2 G0 T9 G1 G2 T10 G3 T11 L3").split()]
SLOT = {step: i for i, step in enumerate(x for x in SCHEDULE if x[0] == "T" or x[0] == "O" and x[1] % 2 == 0)}
SLOTS = len(SLOT)
OH_SLOTS = NO // 2
TR_TABLES = 3
TR_HALF = NG // TR_TABLES
TR_SLOTS = TILES * TR_HALF
G_STEPS = 8
ID_RING = 2
ROW_RING = 8
LANDED = 16 * TR_TABLES
G_BANKS = 4
G_GROUPS = GROUPS // G_BANKS
A_BANKS = -(-F // 8)
PACKS = [(i // 8, (i, i + 2), i // 4 * 4 + 1 + i % 2) for i in range(F - 2) if i % 4 < 2] + \
    [(A_BANKS - 1, (i,), i + 1) for i in (F - 2, F - 1)]
PACK_AT = list(accumulate([len(cols) * (FW - f) for _, cols, f in PACKS], initial=0))
KZ = -(-PACK_AT[-1] // 128)
ZW = KZ * 128
A_USES = A_BANKS + KZ
M_USES = 4
W_LOADS = 16 * (KZ + 6)


def z_inputs():
    rows = []
    for _, cols, f in PACKS:
        for i in cols:
            for j in range(f, FW):
                if j == F:
                    rows.append(D + COLUMNS[i])
                elif j > i:
                    a, b = sorted((COLUMNS[i], COLUMNS[j]))
                    rows.append(D + F + a * (F - 1) - a * (a - 1) // 2 + b - a - 1)
                else:
                    rows.append(-1)
    return rows + [-1] * (ZW - len(rows))


def wait(eng, sem, value):
    if not isinstance(value, int) or value > 0:
        eng.wait_ge(sem, value)


def dlrm_tower(nc, dense_t, ids_gather, ids_one_hot, tables, w1_dense, w1_z, b1, w2, b2, w3, out):
    f32, f32r, i32 = mybir.dt.float32, mybir.dt.float32r, mybir.dt.int32
    ALU, ACT = mybir.AluOpType, mybir.ActivationFunctionType
    ctx = ExitStack()
    with ctx:
        def sb(name, shape, dt=f32):
            return ctx.enter_context(nc.sbuf_tensor(name, shape, dt))

        def banks(name, n):
            return [ctx.enter_context(nc.psum_tensor(f"{name}{i}", [128, 512], f32)) for i in range(n)]

        def sem(name):
            return ctx.enter_context(nc.semaphore(name))

        ident = sb("ident", [128, 128])
        first_row = sb("first_row", [128, 1])
        table_hi = sb("table_hi", [128, NO, KT, D], f32r)
        table_lo = sb("table_lo", [128, NO, KT, D], f32r)
        idx = [sb(f"idx{i}", [128, TILES * NG], i32) for i in range(2)]
        rows = sb("rows", [128, ROW_RING, TR_TABLES, D])
        idb = sb("idb", [128, ID_RING, 2, CH], i32)
        one_hot = [sb(f"one_hot{i}", [128, KT, CH], f32r) for i in range(2)]
        xt = [sb(f"xt{i}", [128, CH]) for i in range(2)]
        et = [sb(f"et{i}", [128, CH * FW]) for i in range(2)]
        gram = sb("gram", [128, GROUPS * F])
        staging = [et[1][:, n * KT * D:(n + 1) * KT * D] for n in range(NO - 2)] + [gram[:, 0:KT * D]]
        table = [t.rearrange("p (k d) -> p k d", k=KT) for t in staging + staging[0:1]]
        w2_raw = staging[1]
        w1_again = staging[2][:, 0:H1]
        z = sb("z", [128, 4, ZW])
        x_parts = [sb(f"x_{part}", [128, CH], f32r) for part in ("hi", "lo")]
        zt_parts = [sb(f"zt_{part}", [128, KZ, CH], f32r) for part in ("hi", "lo")]
        h1_parts = [sb(f"h1_{part}", [128, H1 // 128, CH], f32r) for part in ("hi", "lo")]
        h2 = sb("h2", [128, H2 // 128, CH])
        y = h2[0:1, 0, :]
        w1_parts = [sb(f"w1_{part}", [128, 1 + KZ, H1], f32r) for part in ("hi", "lo")]
        w1_raw = [t[:, :, :].rearrange("p a b -> p (a b)")[:, i * H1:(i + 1) * H1] for t, n in ((z, KZ), (h2, 1))
                  for i in range(n)]
        w2_parts = [sb(f"w2_{part}", [128, H1 // 128, H2], f32r) for part in ("hi", "lo")]
        w3s = sb("w3s", [128, H2 // 128])
        b1s = sb("b1s", [128, H1 // 128])
        b2s = sb("b2s", [128, H2 // 128])

        et_ps = banks("et_ps", 2)
        g_ps = banks("g_ps", 2)
        a_ps = banks("a_ps", 2)
        m_ps = banks("m_ps", 2)

        idx_in = [sem(f"idx_in{i}") for i in range(2)]
        idb_in = [sem(f"idb_in{i}") for i in range(ID_RING)]
        table_in = [sem(f"table_in{n}") for n in range(NO)]
        xt_in = [sem(f"xt_in{i}") for i in range(2)]
        w_in = sem("w_in")
        consts = sem("consts")
        table_hi_done = sem("table_hi_done")
        table_lo_done = sem("table_lo_done")
        w_ready = sem("w_ready")
        z_cleared = sem("z_cleared")
        g_cleared = sem("g_cleared")
        rows_in = [sem(f"rows_in{j}") for j in range(ROW_RING)]
        oh_ready = sem("oh_ready")
        oh_used = sem("oh_used")
        et_done = sem("et_done")
        et_copied = sem("et_copied")
        xt_copied = sem("xt_copied")
        g_done = sem("g_done")
        g_copied = sem("g_copied")
        a_done = sem("a_done")
        a_free = sem("a_free")
        zt_hi_done = sem("zt_hi_done")
        x_hi_done = sem("x_hi_done")
        x_split = sem("x_split")
        m_done = sem("m_done")
        m_free = sem("m_free")
        h1_split = sem("h1_split")
        y_out = sem("y_out")
        waits_apart = sem("waits_apart")

        block = ctx.enter_context(nc.Block())

        def apart(eng):
            eng.sem_inc(waits_apart, 1)

        def phases(eng, phase):
            for p in range(2):
                phase(p, p)
            with eng.Fori(1, NCH // 2) as pair:
                phase(2 * pair, 0)
                phase(2 * pair + 1, 1)
            phase(NCH, NCH % 2)

        def lookup(p):
            return not isinstance(p, int) or p < NCH

        def has_last(p):
            return not isinstance(p, int) or p >= 1

        def gram_chunk(p, n):
            if n < G_STEPS // 2:
                return 0 if lookup(p) else None
            return 1 if has_last(p) else None

        @block.sync
        def _(sp):
            def load_indices(p, par):
                wait(sp, et_done, (p - 2) * SLOTS + SLOT["T", TR_SLOTS - 1] + 1)
                sp.dma_start(idx[par][:, :], ids_gather[bass.ds(p, 1), :, :].rearrange("a p n -> (a p) n"))\
                    .then_inc(idx_in[par], 16)

            def load_ids(p, slots=range(OH_SLOTS)):
                for i in slots:
                    wait(sp, oh_ready, p * NO + 2 * (i - ID_RING) + 2)
                    src = ids_one_hot[bass.ds(p, 1), 2 * i:2 * i + 2, :]
                    sp.dma_start(idb[:, i % ID_RING, :, :], src.broadcast_to([128, 2, CH]))\
                        .then_inc(idb_in[i % ID_RING], 16)

            def load_dense(p, par):
                wait(sp, xt_copied, p - 1)
                wait(sp, x_split, p - 1)
                sp.dma_start(xt[par][:, :], dense_t[:, bass.ds(p * CH, CH)]).then_inc(xt_in[par], 16)

            load_indices(0, 0)
            load_ids(0, [0])
            load_dense(0, 0)
            for n, f in enumerate(ONE_HOT):
                if n >= 2:
                    sp.wait_ge(table_in[n - 2], 32)
                if n == NO - 1:
                    sp.wait_ge(table_lo_done, 1)
                src = tables[f].rearrange("(p k) d -> p k d", k=KT)
                sp.dma_start(table[n][0:SPLIT], src[0:SPLIT]).then_inc(table_in[n], 16)
                sp.dma_start(table[n][SPLIT:KP], src[SPLIT:KP]).then_inc(table_in[n], 16)
                if n == 1:
                    load_ids(0, [1])
            load_ids(0, [2])
            load_dense(1, 1)
            sp.dma_start(w1_raw[0], w1_dense[0:D, :]).then_inc(w_in, 16)
            for k in range(KZ):
                sp.dma_start(w1_raw[1 + k], w1_z[k * 128:(k + 1) * 128, :]).then_inc(w_in, 16)
            load_indices(1, 1)
            load_ids(0, [3])
            sp.dma_start(b1s[:, :], b1).then_inc(w_in, 16)
            sp.dma_start(b2s[:, :], b2).then_inc(w_in, 16)
            sp.dma_start(w3s[:, :], w3).then_inc(w_in, 16)
            sp.wait_ge(table_lo_done, 3)
            sp.dma_start(w1_again, w1_dense[D:, :]).then_inc(w_in, 16)
            sp.dma_start(w2_raw.rearrange("p (k n) -> p k n", n=H2), w2.rearrange("(k p) n -> p k n", p=128))\
                .then_inc(w_in, 16)
            load_ids(1)
            with sp.Fori(1, NCH // 2) as pair:
                for par in range(2):
                    load_indices(2 * pair + par, par)
                    load_dense(2 * pair + par, par)
                    load_ids(2 * pair + par)

        @block.gpsimd
        def _(pool):
            nc.gpsimd.memset(ident[:, :], 0.0).then_inc(consts, 1)
            nc.gpsimd.iota(first_row[:, :], [[0, 1]], base=0, channel_multiplier=KT,
                           allow_small_or_imprecise_dtypes=True).then_inc(consts, 1)
            pool.wait_ge(consts, 2)
            nc.gpsimd.affine_select(out=ident[:, :], in_=ident[:, :], compare_op=ALU.not_equal, fill=1.0,
                                    base=0, pattern=[[-1, 128]], channel_multiplier=1).then_inc(consts, 1)

            def gathers(p, par):
                wait(pool, idx_in[par], (p - par) * 8 + 16)
                for j in range(TR_SLOTS):
                    r = (par * TR_SLOTS + j) % ROW_RING
                    before = SLOT["T", (j - ROW_RING) % TR_SLOTS]
                    wait(pool, et_done, (p * SLOTS if j >= ROW_RING else (p - 1) * SLOTS) + before + 1)
                    apart(pool)
                    t = j // TR_HALF
                    for n in range(TR_TABLES):
                        k = j % TR_HALF * TR_TABLES + n
                        nc.gpsimd.indirect_dma_start(
                            out=rows[:, r, n, :], out_offset=None, in_=tables[GATHERED[k]],
                            in_offset=bass.IndirectOffsetOnAxis(idx[par][:, t * NG + k:t * NG + k + 1], 0))\
                            .then_inc(rows_in[r], 16)

            gathers(0, 0)
            gathers(1, 1)
            with pool.Fori(1, NCH // 2) as pair:
                gathers(2 * pair, 0)
                gathers(2 * pair + 1, 1)

        @block.scalar
        def _(act):
            act.sem_inc(m_free, 2)
            def table_hi_part(n):
                act.wait_ge(table_in[n], 32)
                nc.scalar.copy(table_hi[0:KP, n], table[n][0:KP]).then_inc(table_hi_done, 1)

            for n in range(3):
                table_hi_part(n)

            def phase(p, par):
                if lookup(p):
                    if isinstance(p, int) and p == 1:
                        act.wait_ge(table_lo_done, NO)
                        act.wait_ge(w_ready, 3)
                    wait(act, xt_in[par], (p - par) * 8 + 16)
                    wait(act, g_done, (p - 1) * G_BANKS)
                    e3 = et[par][:, 0:CH * FW].rearrange("d (b f) -> d b f", f=FW)
                    nc.scalar.copy(e3[:, :, F], xt[par][:, :]).then_inc(xt_copied, 1)
                for step in SCHEDULE:
                    kind, n = step
                    if kind == "G" and n % 2 == 1 and gram_chunk(p, n) is not None:
                        bank = n // 2
                        if isinstance(p, int) and p == 0 and n == 1:
                            act.wait_ge(table_lo_done, NO - 1)
                        wait(act, g_done, (p - gram_chunk(p, n)) * G_BANKS + bank + 1)
                        dst = gram[:, :].rearrange("p (f g) -> p g f", f=F)[:, bank * G_GROUPS:(bank + 1) * G_GROUPS, :]
                        src = g_ps[bank % 2][:, 0:G_GROUPS * F].rearrange("p (g f) -> p g f", f=F)
                        nc.scalar.copy(dst, src).then_inc(g_copied, 1)
                    if kind == "L" and n < 2 and has_last(p):
                        if isinstance(p, int) and p == 1 and n == 0:
                            act.wait_ge(w_in, W_LOADS)
                        wait(act, m_done, (p - 1) * M_USES + n + 1)
                        wait(act, y_out, (p - 1) * 16)
                        wait(act, h1_split, (p - 1) * 2 + n)
                        for m in (2 * n, 2 * n + 1):
                            for dst in (h1_parts[0][:, m, :], h2[:, m % 2, :]):
                                last = nc.scalar.activation(dst, m_ps[n][:, m % 2 * CH:m % 2 * CH + CH], ACT.Relu,
                                                            bias=b1s[:, m:m + 1])
                        last.then_inc(m_free, 1)
                    if kind == "Z" and has_last(p):
                        wait(act, a_done, (p - 1) * A_USES + A_BANKS + n + 1)
                        src = a_ps[((1 - par) * A_USES + A_BANKS + n) % 2][:, 0:CH].rearrange("z (q g) -> z q g", q=4)
                        nc.scalar.copy(zt_parts[0][:, n, :].rearrange("z (g q) -> z q g", q=4), src)\
                            .then_inc(zt_hi_done, 1)
                    if kind == "L" and n == 2 and has_last(p):
                        wait(act, m_done, (p - 1) * M_USES + 3)
                        for m in range(2):
                            last = nc.scalar.activation(h2[:, m, :], m_ps[0][:, m * CH:(m + 1) * CH], ACT.Relu,
                                                        bias=b2s[:, m:m + 1])
                        last.then_inc(m_free, 1)
                    if kind == "L" and n == 3 and has_last(p):
                        wait(act, m_done, (p - 1) * M_USES + 4)
                        nc.scalar.copy(y, m_ps[1][0:1, 0:CH]).then_inc(m_free, 1)
                        wait(act, m_free, (p - 1) * M_USES + 4 + 2)
                        act.dma_start(out[:, bass.ds((p - 1) * CH, CH)], y).then_inc(y_out, 16)
                    if isinstance(p, int) and p == 0 and kind == "O" and n < NO - 3:
                        table_hi_part(n + 3)
                    if lookup(p) and (kind == "T" or kind == "O" and n % 2 == 1):
                        s = SLOT[step] if kind == "T" else SLOT["O", n - 1]
                        wait(act, et_done, p * SLOTS + s + 1)
                        if kind == "T":
                            t, f = n // TR_HALF, n % TR_HALF * TR_TABLES
                            at, b, width = slice(f, f + TR_TABLES), slice(t * 128, (t + 1) * 128), TR_TABLES * 128
                        else:
                            at, b, width = slice(NG + n - 1, NG + n + 1), slice(0, CH), 2 * CH
                        dst = e3[:, b, at].rearrange("d b f -> d f b")
                        src = et_ps[(par * SLOTS + s) % 2][:, 0:width].rearrange("d (f b) -> d f b", f=at.stop - at.start)
                        nc.scalar.copy(dst, src).then_inc(et_copied, 1)

            phases(act, phase)
            act.wait_ge(y_out, NCH * 16)

        @block.vector
        def _(dve):
            dve.sem_inc(a_free, 2)
            for bank in g_ps:
                nc.vector.memset(bank[:, 0:G_GROUPS * F], 0.0).then_inc(g_cleared, 1)

            def split_parts(parts, src, hi_done, count, done):
                hi, lo = parts
                nc.vector.tensor_copy(hi, src).then_inc(hi_done, 1)
                dve.wait_ge(hi_done, count)
                nc.vector.tensor_tensor(lo, src, hi.bitcast(f32), ALU.subtract).then_inc(done, 1)

            dve.wait_ge(consts, 3)

            def build(p, n):
                if isinstance(p, int) and p == 0:
                    dve.wait_ge(table_hi_done, n + 1)
                    nc.vector.tensor_tensor(table_lo[0:KP, n], table[n][0:KP], table_hi[0:KP, n].bitcast(f32),
                                            ALU.subtract).then_inc(table_lo_done, 1)
                if n % 2 == 0:
                    wait(dve, idb_in[n // 2 % ID_RING], (p * (OH_SLOTS // ID_RING) + n // 2 // ID_RING + 1) * 16)
                    wait(dve, oh_used, p * OH_SLOTS + n // 2)
                else:
                    before = (p * SLOTS if n > 1 else (p - 1) * SLOTS) + SLOT["O", (n - 3) % NO]
                    wait(dve, et_done, before + 1)
                for k in range(KT):
                    last = nc.vector.tensor_scalar(one_hot[n % 2][0:KP, k, :], idb[0:KP, n // 2 % ID_RING, n % 2, :],
                                                   first_row[0:KP, 0:1], float(k), ALU.subtract, ALU.is_equal)
                last.then_inc(oh_ready, 1)

            def phase(p, par):
                if isinstance(p, int) and p == 1:
                    dve.wait_ge(w_in, W_LOADS)
                    split_parts([t[:, :, :] for t in w2_parts], w2_raw.rearrange("p (k n) -> p k n", n=H2),
                                w_ready, 1, w_ready)
                    nc.vector.tensor_tensor(w1_raw[0], w1_raw[0], w1_again, ALU.add).then_inc(w_ready, 1)
                    dve.wait_ge(w_ready, 3)
                    for k in range(1 + KZ):
                        split_parts([t[:, k, :] for t in w1_parts], w1_raw[k], w_ready, 2 * k + 4, w_ready)
                    nc.vector.memset(z[0:GROUPS, :, PACK_AT[-1]:ZW], 0.0).then_inc(z_cleared, 1)
                if lookup(p):
                    build(p, 0)
                    build(p, 1)
                for kind, n in SCHEDULE:
                    if has_last(p):
                        a0 = (p - 1) * A_USES
                        a_bank = a_ps[((1 - par) * A_USES + (A_BANKS if kind == "Z" else 0) + n) % 2]
                        if kind == "G" and n == G_STEPS // 2:
                            wait(dve, et_done, (p - 1) * SLOTS)
                            split_parts([t[:, :] for t in x_parts], xt[1 - par][:, :], x_hi_done, p, x_split)
                        if kind == "A":
                            wait(dve, a_done, a0 + n + 1)
                            for at, (bank, cols, f) in zip(PACK_AT, PACKS):
                                if bank == n:
                                    half = cols[0] % 2 * GROUPS
                                    i = cols[0] % 8 // 2
                                    dst = z[0:GROUPS, :, at:at + len(cols) * (FW - f)]
                                    src = a_bank[half:half + GROUPS, :].rearrange("g (i q f) -> g i q f", i=4, q=4)
                                    last = nc.vector.tensor_copy(
                                        dst.rearrange("g q (i f) -> g i q f", i=len(cols)),
                                        src[:, i:i + len(cols), :, f:FW])
                            last.then_inc(a_free, 1)
                        if kind == "Z":
                            wait(dve, zt_hi_done, (p - 1) * KZ + n + 1)
                            hi, lo = [t[:, n, :].rearrange("z (g q) -> z q g", q=4) for t in zt_parts]
                            nc.vector.tensor_tensor(lo, a_bank[:, 0:CH].rearrange("z (q g) -> z q g", q=4),
                                                    hi.bitcast(f32), ALU.subtract).then_inc(a_free, 1)
                        if kind == "L" and n < 2:
                            wait(dve, m_free, (p - 1) * M_USES + n + 1 + 2)
                            half = slice(2 * n, 2 * n + 2)
                            nc.vector.tensor_tensor(h1_parts[1][:, half, :], h2[:, :, :],
                                                    h1_parts[0][:, half, :].bitcast(f32), ALU.subtract)\
                                .then_inc(h1_split, 1)
                    if lookup(p) and kind == "B":
                        build(p, n)

            phases(dve, phase)

        @block.tensor
        def _(pe):
            pe.wait_ge(consts, 3)
            pe.wait_ge(g_cleared, 2)

            def phase(p, par):
                for step in SCHEDULE:
                    kind, n = step
                    if kind == "G" and gram_chunk(p, n) is not None:
                        bank = n // 2
                        back = gram_chunk(p, n)
                        if n == 0:
                            last_slot = max(SLOT["T", TR_HALF - 1], SLOT["O", NO - 2])
                            wait(pe, et_copied, p * SLOTS + last_slot + 1)
                            wait(pe, xt_copied, p + 1)
                        if n == G_STEPS // 2:
                            wait(pe, et_copied, p * SLOTS)
                        if n % 2 == 0:
                            wait(pe, g_copied, (p - back) * G_BANKS + bank - 1)
                        e = et[(par + back) % 2]
                        for grp in range(n * GROUPS // G_STEPS, (n + 1) * GROUPS // G_STEPS):
                            for q in range(4):
                                b, c = (4 * grp + q) * FW, grp % G_GROUPS * F
                                last = nc.tensor.matmul(g_ps[bank % 2][32 * q:32 * q + FW, c:c + F], e[:, b:b + FW],
                                                        e[:, b:b + F], start=True, stop=True)
                        if n % 2 == 1:
                            last.then_inc(g_done, 1)
                    if kind == "A" and has_last(p):
                        a0 = (p - 1) * A_USES
                        if n == 0:
                            wait(pe, g_copied, p * G_BANKS)
                        wait(pe, a_free, a0 + n + 1)
                        a_bank = a_ps[((1 - par) * A_USES + n) % 2]
                        apart(pe)
                        for i in range(8 * n, min(8 * n + 8, F), 2):
                            last = nc.tensor.transpose(a_bank[:, i % 8 * 64:i % 8 * 64 + 128],
                                                       gram[:, i * GROUPS:(i + 2) * GROUPS], ident[:, :])
                        last.then_inc(a_done, 1)
                    if kind == "Z" and has_last(p):
                        wait(pe, z_cleared, 1)
                        wait(pe, a_free, (p - 1) * A_USES + A_BANKS + max(n + 1, 2))
                        apart(pe)
                        a_bank = a_ps[((1 - par) * A_USES + A_BANKS + n) % 2]
                        for q in range(4):
                            last = nc.tensor.transpose(a_bank[:, q * GROUPS:(q + 1) * GROUPS],
                                                       z[0:GROUPS, q, n * 128:(n + 1) * 128],
                                                       ident[0:GROUPS, 0:GROUPS])
                        last.then_inc(a_done, 1)
                    if kind == "L" and n < 2 and has_last(p):
                        if isinstance(p, int) and p == 1 and n == 0:
                            pe.wait_ge(w_ready, 3 + 2 * (1 + KZ))
                        wait(pe, m_free, (p - 1) * M_USES + n + 1)
                        wait(pe, x_split, p)
                        for m in (2 * n, 2 * n + 1):
                            dst = m_ps[n][:, m % 2 * CH:m % 2 * CH + CH]
                            for k in range(1 + KZ):
                                if m == 0 and k > 0:
                                    wait(pe, a_free, (p - 1) * A_USES + A_BANKS + k + 2)
                                for a, b in ((0, 0), (1, 0), (0, 1)):
                                    rhs = zt_parts[b][:, k - 1, :] if k else x_parts[b][:, :]
                                    last = nc.tensor.matmul(dst, w1_parts[a][:, k, m * 128:(m + 1) * 128],
                                                            rhs, start=k == 0 and (a, b) == (0, 0),
                                                            stop=k == KZ and (a, b) == (0, 1))
                        last.then_inc(m_done, 1)
                    if kind == "L" and n == 2 and has_last(p):
                        wait(pe, m_free, (p - 1) * M_USES + 2 + 1)
                        for m in range(2):
                            for k in range(4):
                                if m == 0 and k % 2 == 0:
                                    wait(pe, h1_split, (p - 1) * 2 + k // 2 + 1)
                                for a, b in ((0, 0), (1, 0), (0, 1)):
                                    last = nc.tensor.matmul(m_ps[0][:, m * CH:(m + 1) * CH],
                                                            w2_parts[a][:, k, m * 128:(m + 1) * 128],
                                                            h1_parts[b][:, k, :],
                                                            start=k == 0 and (a, b) == (0, 0),
                                                            stop=k == 3 and (a, b) == (0, 1))
                        last.then_inc(m_done, 1)
                    if kind == "L" and n == 3 and has_last(p):
                        wait(pe, m_free, (p - 1) * M_USES + 3 + 2)
                        for k in range(H2 // 128):
                            last = nc.tensor.matmul(m_ps[1][0:1, 0:CH], w3s[:, k:k + 1], h2[:, k, :],
                                                    start=k == 0, stop=k == H2 // 128 - 1)
                        last.then_inc(m_done, 1)
                    if lookup(p) and kind == "T":
                        s = SLOT[step]
                        use, r = divmod(par * TR_SLOTS + n, ROW_RING)
                        ps = et_ps[(par * SLOTS + s) % 2]
                        wait(pe, et_copied, p * SLOTS + s - 1)
                        wait(pe, rows_in[r], (p - par) * (TR_SLOTS * LANDED // ROW_RING) + (use + 1) * LANDED)
                        for i in range(TR_TABLES):
                            last = nc.tensor.transpose(ps[:, i * 128:(i + 1) * 128], rows[:, r, i, :], ident[:, :])
                        last.then_inc(et_done, 1)
                    if lookup(p) and kind == "O":
                        s = SLOT["O", n // 2 * 2]
                        ps = et_ps[(par * SLOTS + s) % 2]
                        if n % 2 == 0:
                            wait(pe, et_copied, p * SLOTS + s - 1)
                        wait(pe, oh_ready, p * NO + n + 1)
                        for k in range(KT):
                            for part in (table_hi, table_lo):
                                last = nc.tensor.matmul(ps[:, n % 2 * CH:n % 2 * CH + CH], part[0:KP, n, k, :],
                                                        one_hot[n % 2][0:KP, k, :],
                                                        start=k == 0 and part is table_hi,
                                                        stop=k == KT - 1 and part is table_lo)
                        last.then_inc((oh_used, et_done)[n % 2], 1)

            phases(pe, phase)


def kernel(**inputs):
    import numpy as np
    import concourse.bacc as bacc
    from concourse.bass_utils import run_bass_kernel_spmd

    nc = bacc.Bacc("TRN2", target_bir_lowering=False, num_devices=1)
    arrays = {}

    def give(name, a):
        a = np.ascontiguousarray(a)
        arrays[name] = a
        return nc.dram_tensor(name, a.shape, mybir.dt.from_np(a.dtype), kind="ExternalInput").ap()

    ids = np.asarray(inputs["ids"])
    gather = ids[:, list(GATHERED)].reshape(NCH, TILES, 128, NG).transpose(0, 2, 1, 3).reshape(NCH, 128, TILES * NG)
    one_hot = ids[:, list(ONE_HOT)].reshape(NCH, CH, NO).transpose(0, 2, 1)
    w1 = np.asarray(inputs["W_top1"])
    z_rows = np.array(z_inputs())
    w1_z = np.zeros((ZW, H1), w1.dtype)
    w1_z[z_rows >= 0] = w1[z_rows[z_rows >= 0]]
    args = [
        give("dense_t", np.asarray(inputs["r_dense_features"]).T),
        give("ids_gather", gather),
        give("ids_one_hot", one_hot),
        [give(f"tbl_{f}_in", np.asarray(inputs[f"tbl_{f}"])) for f in range(F)],
        give("w1_dense", np.concatenate([w1[:D], w1[D + F + NPAIR:]])),
        give("w1_z", w1_z),
        give("b1", np.asarray(inputs["b_top1"]).reshape(H1 // 128, 128).T),
        give("w2", np.asarray(inputs["W_top2"])),
        give("b2", np.asarray(inputs["b_top2"]).reshape(H2 // 128, 128).T),
        give("w3", np.asarray(inputs["W_top3"]).reshape(H2 // 128, 128).T),
    ]
    out = nc.dram_tensor("out", (1, B), mybir.dt.float32, kind="ExternalOutput").ap()
    dlrm_tower(nc, *args, out)
    r = run_bass_kernel_spmd(nc, [arrays], core_ids=[0])
    return r.results[0]["out"].reshape(B, 1)
```
